# Optimizing a Trainium2 kernel written in Bass

```python
import numpy as np
import jax
import jax.numpy as jnp

def _softmax(x, axis=-1):
    return jax.nn.softmax(x, axis=axis)

def _gelu(x):
    return jax.nn.gelu(x, approximate=True)

def _silu(x):
    return jax.nn.silu(x)

def _sigmoid(x):
    return jax.nn.sigmoid(x)

def _layernorm(x, axis=-1, eps=1e-05):
    m = jnp.mean(x, axis=axis, keepdims=True)
    v = jnp.var(x, axis=axis, keepdims=True)
    return (x - m) / jnp.sqrt(v + eps)

def _scatter_add(tgt, idx, src, axis=0):
    return tgt.at[idx].add(src)

def _segment_sum(src, seg, n):
    return jax.ops.segment_sum(src, seg, n)
kernel_name = 'mk_dlrm_tower_d1_rec_r8_15f584'

def setup_inputs(seed: int=0):
    np.random.seed(seed)
    _w = jnp.asarray

    def _rec_inputs():
        import jax
        import jax.numpy as jnp
        _tk = jax.random.key(seed)
        dense_ctx = jax.random.normal(jax.random.fold_in(_tk, 190), (512, 16), jnp.float32)
        ids = jnp.stack([jax.random.randint(jax.random.fold_in(_tk, 200 + f), (512,), 0, v, jnp.int32) for f, v in enumerate([1000, 12500, 1250, 1250, 1250, 1000, 12500, 12500, 1000, 1000, 1250, 1250, 12500, 1000, 1250, 12500, 12500, 1000, 1250, 1000, 12500, 12500, 1000, 1250, 1250, 1000, 1250, 1000, 1000, 1000, 1000, 1250])], axis=1)
        tbl_0 = 0.05 * jax.random.normal(jax.random.fold_in(_tk, 500 + 0), (1000, 256), jnp.float32)
        tbl_1 = 0.05 * jax.random.normal(jax.random.fold_in(_tk, 500 + 1), (12500, 256), jnp.float32)
        tbl_2 = 0.05 * jax.random.normal(jax.random.fold_in(_tk, 500 + 2), (1250, 256), jnp.float32)
        tbl_3 = 0.05 * jax.random.normal(jax.random.fold_in(_tk, 500 + 3), (1250, 256), jnp.float32)
        tbl_4 = 0.05 * jax.random.normal(jax.random.fold_in(_tk, 500 + 4), (1250, 256), jnp.float32)
        tbl_5 = 0.05 * jax.random.normal(jax.random.fold_in(_tk, 500 + 5), (1000, 256), jnp.float32)
        tbl_6 = 0.05 * jax.random.normal(jax.random.fold_in(_tk, 500 + 6), (12500, 256), jnp.float32)
        tbl_7 = 0.05 * jax.random.normal(jax.random.fold_in(_tk, 500 + 7), (12500, 256), jnp.float32)
        tbl_8 = 0.05 * jax.random.normal(jax.random.fold_in(_tk, 500 + 8), (1000, 256), jnp.float32)
        tbl_9 = 0.05 * jax.random.normal(jax.random.fold_in(_tk, 500 + 9), (1000, 256), jnp.float32)
        tbl_10 = 0.05 * jax.random.normal(jax.random.fold_in(_tk, 500 + 10), (1250, 256), jnp.float32)
        tbl_11 = 0.05 * jax.random.normal(jax.random.fold_in(_tk, 500 + 11), (1250, 256), jnp.float32)
        tbl_12 = 0.05 * jax.random.normal(jax.random.fold_in(_tk, 500 + 12), (12500, 256), jnp.float32)
        tbl_13 = 0.05 * jax.random.normal(jax.random.fold_in(_tk, 500 + 13), (1000, 256), jnp.float32)
        tbl_14 = 0.05 * jax.random.normal(jax.random.fold_in(_tk, 500 + 14), (1250, 256), jnp.float32)
        tbl_15 = 0.05 * jax.random.normal(jax.random.fold_in(_tk, 500 + 15), (12500, 256), jnp.float32)
        tbl_16 = 0.05 * jax.random.normal(jax.random.fold_in(_tk, 500 + 16), (12500, 256), jnp.float32)
        tbl_17 = 0.05 * jax.random.normal(jax.random.fold_in(_tk, 500 + 17), (1000, 256), jnp.float32)
        tbl_18 = 0.05 * jax.random.normal(jax.random.fold_in(_tk, 500 + 18), (1250, 256), jnp.float32)
        tbl_19 = 0.05 * jax.random.normal(jax.random.fold_in(_tk, 500 + 19), (1000, 256), jnp.float32)
        tbl_20 = 0.05 * jax.random.normal(jax.random.fold_in(_tk, 500 + 20), (12500, 256), jnp.float32)
        tbl_21 = 0.05 * jax.random.normal(jax.random.fold_in(_tk, 500 + 21), (12500, 256), jnp.float32)
        tbl_22 = 0.05 * jax.random.normal(jax.random.fold_in(_tk, 500 + 22), (1000, 256), jnp.float32)
        tbl_23 = 0.05 * jax.random.normal(jax.random.fold_in(_tk, 500 + 23), (1250, 256), jnp.float32)
        tbl_24 = 0.05 * jax.random.normal(jax.random.fold_in(_tk, 500 + 24), (1250, 256), jnp.float32)
        tbl_25 = 0.05 * jax.random.normal(jax.random.fold_in(_tk, 500 + 25), (1000, 256), jnp.float32)
        tbl_26 = 0.05 * jax.random.normal(jax.random.fold_in(_tk, 500 + 26), (1250, 256), jnp.float32)
        tbl_27 = 0.05 * jax.random.normal(jax.random.fold_in(_tk, 500 + 27), (1000, 256), jnp.float32)
        tbl_28 = 0.05 * jax.random.normal(jax.random.fold_in(_tk, 500 + 28), (1000, 256), jnp.float32)
        tbl_29 = 0.05 * jax.random.normal(jax.random.fold_in(_tk, 500 + 29), (1000, 256), jnp.float32)
        tbl_30 = 0.05 * jax.random.normal(jax.random.fold_in(_tk, 500 + 30), (1000, 256), jnp.float32)
        tbl_31 = 0.05 * jax.random.normal(jax.random.fold_in(_tk, 500 + 31), (1250, 256), jnp.float32)
        _rk = jax.random.fold_in(_tk, 7)
        W_top1 = 0.0441942 * jax.random.normal(jax.random.fold_in(_tk, 801), (512, 512), jnp.float32)
        W_top2 = 0.0441942 * jax.random.normal(jax.random.fold_in(_tk, 802), (512, 256), jnp.float32)
        W_top3 = 0.0625 * jax.random.normal(jax.random.fold_in(_tk, 803), (256, 1), jnp.float32)
        b_top1 = jnp.zeros((512,), jnp.float32)
        b_top2 = jnp.zeros((256,), jnp.float32)
        return (dense_ctx, ids, tbl_0, tbl_1, tbl_2, tbl_3, tbl_4, tbl_5, tbl_6, tbl_7, tbl_8, tbl_9, tbl_10, tbl_11, tbl_12, tbl_13, tbl_14, tbl_15, tbl_16, tbl_17, tbl_18, tbl_19, tbl_20, tbl_21, tbl_22, tbl_23, tbl_24, tbl_25, tbl_26, tbl_27, tbl_28, tbl_29, tbl_30, tbl_31, W_top1, b_top1, W_top2, b_top2, W_top3)
    dense_ctx, ids, tbl_0, tbl_1, tbl_2, tbl_3, tbl_4, tbl_5, tbl_6, tbl_7, tbl_8, tbl_9, tbl_10, tbl_11, tbl_12, tbl_13, tbl_14, tbl_15, tbl_16, tbl_17, tbl_18, tbl_19, tbl_20, tbl_21, tbl_22, tbl_23, tbl_24, tbl_25, tbl_26, tbl_27, tbl_28, tbl_29, tbl_30, tbl_31, W_top1, b_top1, W_top2, b_top2, W_top3 = _rec_inputs()

    def _L0_rec_setup():
        import jax, jax.numpy as jnp
        import numpy as np
        B, N, D = (1024, 32, 256)
        key = jax.random.key(seed)
        x = jax.random.normal(key, (B, N, D), dtype=jnp.float32)
        return {'x': x}
    _L0_rec_all = _L0_rec_setup()
    _L0_rec_in = {k: v for k, v in _L0_rec_all.items() if k in ()}
    del _L0_rec_all
    return {'dense_ctx': dense_ctx, 'ids': ids, 'tbl_0': tbl_0, 'tbl_1': tbl_1, 'tbl_2': tbl_2, 'tbl_3': tbl_3, 'tbl_4': tbl_4, 'tbl_5': tbl_5, 'tbl_6': tbl_6, 'tbl_7': tbl_7, 'tbl_8': tbl_8, 'tbl_9': tbl_9, 'tbl_10': tbl_10, 'tbl_11': tbl_11, 'tbl_12': tbl_12, 'tbl_13': tbl_13, 'tbl_14': tbl_14, 'tbl_15': tbl_15, 'tbl_16': tbl_16, 'tbl_17': tbl_17, 'tbl_18': tbl_18, 'tbl_19': tbl_19, 'tbl_20': tbl_20, 'tbl_21': tbl_21, 'tbl_22': tbl_22, 'tbl_23': tbl_23, 'tbl_24': tbl_24, 'tbl_25': tbl_25, 'tbl_26': tbl_26, 'tbl_27': tbl_27, 'tbl_28': tbl_28, 'tbl_29': tbl_29, 'tbl_30': tbl_30, 'tbl_31': tbl_31, 'W_top1': W_top1, 'b_top1': b_top1, 'W_top2': W_top2, 'b_top2': b_top2, 'W_top3': W_top3}

def reference(dense_ctx, ids, tbl_0, tbl_1, tbl_2, tbl_3, tbl_4, tbl_5, tbl_6, tbl_7, tbl_8, tbl_9, tbl_10, tbl_11, tbl_12, tbl_13, tbl_14, tbl_15, tbl_16, tbl_17, tbl_18, tbl_19, tbl_20, tbl_21, tbl_22, tbl_23, tbl_24, tbl_25, tbl_26, tbl_27, tbl_28, tbl_29, tbl_30, tbl_31, W_top1, b_top1, W_top2, b_top2, W_top3):
    import jax
    import jax.numpy as jnp

    def _L0_rec_ref(x):
        import jax, jax.numpy as jnp
        import numpy as np
        B, N, D = (1024, 32, 256)
        'Second-order feature interaction (DLRM dot interaction).\n\n            Computes dot(x_i, x_j) for all field pairs i < j (self_interaction=False),\n            flattened in row-major upper-triangular order -> [B, N*(N-1)/2].\n            Matches tf.boolean_mask(dot_products, strictly_upper_mask) ordering.\n            '
        b, n, d = x.shape
        iu, ju = jnp.triu_indices(n, k=1)
        dots = jnp.einsum('bnd,bmd->bnm', x, x)
        return dots[:, iu, ju]
    e = jnp.stack([tbl_0[ids[:, 0]], tbl_1[ids[:, 1]], tbl_2[ids[:, 2]], tbl_3[ids[:, 3]], tbl_4[ids[:, 4]], tbl_5[ids[:, 5]], tbl_6[ids[:, 6]], tbl_7[ids[:, 7]], tbl_8[ids[:, 8]], tbl_9[ids[:, 9]], tbl_10[ids[:, 10]], tbl_11[ids[:, 11]], tbl_12[ids[:, 12]], tbl_13[ids[:, 13]], tbl_14[ids[:, 14]], tbl_15[ids[:, 15]], tbl_16[ids[:, 16]], tbl_17[ids[:, 17]], tbl_18[ids[:, 18]], tbl_19[ids[:, 19]], tbl_20[ids[:, 20]], tbl_21[ids[:, 21]], tbl_22[ids[:, 22]], tbl_23[ids[:, 23]], tbl_24[ids[:, 24]], tbl_25[ids[:, 25]], tbl_26[ids[:, 26]], tbl_27[ids[:, 27]], tbl_28[ids[:, 28]], tbl_29[ids[:, 29]], tbl_30[ids[:, 30]], tbl_31[ids[:, 31]]], axis=1)
    z = _L0_rec_ref(e)
    z = z.reshape(z.shape[0], -1)
    h = jnp.concatenate([z, dense_ctx], axis=1)
    h = jnp.maximum(h @ W_top1 + b_top1, 0.0)
    h = jnp.maximum(h @ W_top2 + b_top2, 0.0)
    y = h @ W_top3
    return y

_drawn_inputs = setup_inputs


def setup_inputs(seed=0):
    import zlib

    import numpy as np

    out = dict(_drawn_inputs(seed))
    spreads = {'b_top1': (0.0, 0.1), 'b_top2': (0.0, 0.1)}
    factors = {}
    for name, (base, spread) in spreads.items():
        noise = np.random.default_rng([zlib.crc32(name.encode()), seed]).standard_normal(out[name].shape)
        drawn = base * np.exp(spread * noise) if base else spread * noise
        out[name] = jnp.asarray(drawn.astype(out[name].dtype))
    for name, factor in factors.items():
        out[name] = (out[name] * factor).astype(out[name].dtype)
    return out
```

```python
from contextlib import ExitStack

import numpy as np

import concourse.bass as bass
from concourse import mybir

F32 = mybir.dt.float32
I32 = mybir.dt.int32
ALU = mybir.AluOpType
ACT = mybir.ActivationFunctionType

P = 128
Q = 32
N_FIELDS = 32
GROUP = P // N_FIELDS
BLOCK = 128
GROUPS = BLOCK // GROUP
PAIRS = GROUPS // 2
SLOTS = 16
BATCH = 8
BATCHES = GROUPS // BATCH
PER_BATCH = BATCH // 2
XT_SLOTS = 4
QUADS = P // Q
JJ = N_FIELDS // QUADS


def build_tower(nc, table, ids, base, dense, w1, b1, w2, b2, w3, out):
    D = table.shape[1]
    DC = D // P
    B = out.shape[1]
    NB = B // BLOCK
    H1 = w1.shape[2]
    H2 = w2.shape[2]
    N1, N2 = H1 // P, H2 // P
    assert N_FIELDS == Q and GROUP == QUADS and NB * BLOCK == B

    with ExitStack() as ctx:
        def sb(name, shape, dt=F32):
            return ctx.enter_context(nc.sbuf_tensor(name, shape, dt))

        def bank(name):
            return ctx.enter_context(nc.psum_tensor(name, [P, 512], F32))

        def sem(name):
            return ctx.enter_context(nc.semaphore(name))

        ids_sb = sb("ids_sb", [P, ids.shape[1]], I32)
        base_sb = sb("base_sb", [P, 1], I32)
        row_ids = sb("row_ids", [P, ids.shape[1]], I32)
        zeros = sb("zeros", [P, P])
        ident = sb("ident", [P, P])
        rows = sb("rows", [P, SLOTS, D])
        xt = sb("xt", [P, XT_SLOTS, 2, DC, P])
        pairs = sb("pairs", [P, JJ, BLOCK])
        w1_sb = sb("w1_sb", [P, JJ, H1])
        w2_sb = sb("w2_sb", [P, N1, H2])
        w3_sb = sb("w3_sb", [P, N2])
        b1_sb = sb("b1_sb", [P, N1])
        b2_sb = sb("b2_sb", [P, N2])
        h1 = sb("h1", [P, N1, BLOCK])
        h2 = sb("h2", [P, N2, BLOCK])
        y = sb("y", [1, B])

        xt_ps = [bank(f"xt_ps{n}") for n in range(2)]
        dots_ps = [ctx.enter_context(nc.psum_tensor(f"dots_ps{n}", [P, BATCH, P], F32)) for n in range(2)]
        mlp_ps = [bank(f"mlp_ps{n}") for n in range(2)]

        ids_in = sem("ids_in")
        weights_in = sem("weights_in")
        small_in = sem("small_in")
        dense_in = sem("dense_in")
        zeros_set = sem("zeros_set")
        ident_set = sem("ident_set")
        pairs_zeroed = sem("pairs_zeroed")
        ids_ready = sem("ids_ready")
        gathered = [sem(f"gathered{n}") for n in range(SLOTS)]
        transposed = sem("transposed")
        xt_moved = sem("xt_moved")
        dots_done = sem("dots_done")
        dots_moved = sem("dots_moved")
        l1_done = sem("l1_done")
        h1_ready = sem("h1_ready")
        l2_done = sem("l2_done")
        h2_ready = sem("h2_ready")
        l3_done = sem("l3_done")
        y_ready = sem("y_ready")
        stored = sem("stored")

        dense_rows = [pairs[Q * q + Q - 1:Q * q + Q, :, :] for q in range(dense.shape[1])]

        block = ctx.enter_context(nc.Block())

        @block.sync
        def _(sp):
            sp.dma_start(ids_sb[:], ids).then_inc(ids_in, 16)
            sp.dma_start(w1_sb[:], w1).then_inc(weights_in, 16)
            sp.dma_start(w2_sb[:], w2).then_inc(weights_in, 16)

            def dense_of(b, q):
                sp.dma_start(dense_rows[q], dense[b, q]).then_inc(dense_in, 16)

            sp.wait_ge(pairs_zeroed, 1)
            for q in range(len(dense_rows)):
                dense_of(0, q)
            with sp.Fori(1, NB) as b:
                sp.wait_ge(l1_done, N1 * b)
                for q in range(len(dense_rows)):
                    sp.dma_start(dense_rows[q], dense[bass.ds(b, 1), q]).then_inc(dense_in, 16)
            sp.wait_ge(y_ready, NB)
            sp.dma_start(out, y[:]).then_inc(stored, 16)
            sp.wait_ge(stored, 16)

        @block.gpsimd
        def _(pool):
            nc.gpsimd.memset(zeros[:], 0.0).then_inc(zeros_set, 1)
            pool.wait_ge(zeros_set, 1)
            nc.gpsimd.affine_select(out=ident[:], in_=zeros[:], compare_op=ALU.not_equal, fill=1.0, base=0,
                                    pattern=[[-1, P]], channel_multiplier=1).then_inc(ident_set, 1)

            def gather(g, source):
                nc.gpsimd.indirect_dma_start(
                    rows[:, g % SLOTS, :], None, table,
                    bass.IndirectOffsetOnAxis(ap=source[:, g:g + 1], axis=0)).then_inc(gathered[g % SLOTS], 16)

            pool.wait_ge(ids_ready, 1)
            for g in range(NB * GROUPS):
                if g >= SLOTS and g % 2 == 0:
                    pool.wait_ge(transposed, (g - SLOTS) // 2 + 1)
                nc.gpsimd.indirect_dma_start(
                    rows[:, g % SLOTS, :], None, table,
                    bass.IndirectOffsetOnAxis(ap=row_ids[:, g:g + 1], axis=0)).then_inc(gathered[g % SLOTS], 16)

        @block.vector
        def _(dve):
            dve.wait_ge(ids_in, 32)
            nc.vector.tensor_tensor(row_ids[:], ids_sb[:], base_sb[:, 0:1].to_broadcast([P, ids.shape[1]]),
                                    ALU.add).then_inc(ids_ready, 1)
            nc.vector.memset(pairs[:], 0.0).then_inc(pairs_zeroed, 1)

            def move_batch(n):
                for s in range(GROUP):
                    for q in range(QUADS):
                        col = s * Q + n * BATCH
                        last = nc.vector.tensor_copy(
                            pairs[Q * q:Q * q + Q - 1, :, col:col + BATCH],
                            dots_ps[n % 2][Q * s:Q * s + Q - 1, :, Q * s + JJ * q:Q * s + JJ * (q + 1)]
                            .rearrange("i g j -> i j g"))
                last.then_inc(dots_moved, 1)

            dve.wait_ge(pairs_zeroed, 1)
            for n in range(BATCHES):
                dve.wait_ge(dots_done, n + 1)
                move_batch(n)
            with dve.Fori(1, NB) as b:
                for n in range(BATCHES):
                    if n == 0:
                        dve.wait_ge(l1_done, N1 * b)
                    dve.wait_ge(dots_done, b * BATCHES + (n + 1))
                    move_batch(n)

        @block.scalar
        def _(act):
            act.dma_start(base_sb[:], base).then_inc(ids_in, 16)
            act.dma_start(b1_sb[:], b1).then_inc(small_in, 16)
            act.dma_start(b2_sb[:], b2).then_inc(small_in, 16)
            act.dma_start(w3_sb[:], w3).then_inc(small_in, 16)

            def move_xt(b, p):
                act.wait_ge(transposed, b * PAIRS + (p + 1))
                nc.scalar.copy(xt[:, p % XT_SLOTS, :, :, :].rearrange("d g c n -> d (g c n)"),
                               xt_ps[p % 2][:]).then_inc(xt_moved, 1)

            def relu1(b):
                for n in range(N1):
                    act.wait_ge(l1_done, b * N1 + (n + 1))
                    nc.scalar.activation(h1[:, n, :], mlp_ps[n % 2][:, 0:BLOCK], ACT.Relu,
                                         bias=b1_sb[:, n:n + 1]).then_inc(h1_ready, 1)

            def relu2(b):
                for n in range(N2):
                    act.wait_ge(l2_done, b * N2 + (n + 1))
                    nc.scalar.activation(h2[:, n, :], mlp_ps[n % 2][:, 0:BLOCK], ACT.Relu,
                                         bias=b2_sb[:, n:n + 1]).then_inc(h2_ready, 1)

            def keep_y(b):
                act.wait_ge(l3_done, b + 1)
                nc.scalar.copy(y[:, bass.ds(b * BLOCK, BLOCK)], mlp_ps[0][0:1, 0:BLOCK]).then_inc(y_ready, 1)

            for p in range(PAIRS):
                if p >= XT_SLOTS and p % PER_BATCH == 0:
                    act.wait_ge(dots_done, p // PER_BATCH)
                move_xt(0, p)
            act.wait_ge(small_in, 48)
            with act.Fori(1, NB) as b:
                for p in range(PAIRS):
                    if p % PER_BATCH == 0:
                        act.wait_ge(dots_done, b * BATCHES + p // PER_BATCH)
                    move_xt(b, p)
                    if p == PER_BATCH:
                        relu1(b - 1)
                    if p == PER_BATCH + 1:
                        relu2(b - 1)
                    if p == PER_BATCH + 2:
                        keep_y(b - 1)
            relu1(NB - 1)
            relu2(NB - 1)
            act.wait_ge(l3_done, NB)
            nc.scalar.copy(y[:, (NB - 1) * BLOCK:], mlp_ps[0][0:1, 0:BLOCK]).then_inc(y_ready, 1)

        @block.tensor
        def _(pe):
            def transpose_two(b, p, first):
                if not (first and p < 2):
                    pe.wait_ge(xt_moved, b * PAIRS + (p - 1))
                for g in range(2):
                    slot = (2 * p + g) % SLOTS
                    turn = (2 * p + g) // SLOTS
                    pe.wait_ge(gathered[slot], b * (16 * GROUPS // SLOTS) + 16 * (turn + 1))
                    for c in range(DC):
                        last = nc.tensor.transpose(xt_ps[p % 2][:, (g * DC + c) * P:(g * DC + c + 1) * P],
                                                   rows[:, slot, c * P:(c + 1) * P], ident[:])
                last.then_inc(transposed, 1)

            def dot_two(b, p, first):
                n = p // PER_BATCH
                pe.wait_ge(xt_moved, b * PAIRS + (p + 1))
                if p % PER_BATCH == 0 and not (first and n < 2):
                    pe.wait_ge(dots_moved, b * BATCHES + (n - 1))
                for g in range(2):
                    at = (2 * p + g) % BATCH
                    for c in range(DC):
                        x = xt[:, p % XT_SLOTS, g, c, :]
                        last = nc.tensor.matmul(dots_ps[n % 2][:, at, :], x, x, start=(c == 0), stop=(c == DC - 1))
                if p % PER_BATCH == PER_BATCH - 1:
                    last.then_inc(dots_done, 1)

            def layer1(b):
                pe.wait_ge(dots_moved, BATCHES * (b + 1))
                pe.wait_ge(dense_in, 16 * len(dense_rows) * (b + 1))
                for n in range(N1):
                    if n >= 2:
                        pe.wait_ge(h1_ready, b * N1 + (n - 1))
                    for j in range(JJ):
                        last = nc.tensor.matmul(mlp_ps[n % 2][:, 0:BLOCK], w1_sb[:, j, n * P:(n + 1) * P],
                                                pairs[:, j, :], start=(j == 0), stop=(j == JJ - 1))
                    last.then_inc(l1_done, 1)

            def layer2(b):
                pe.wait_ge(h1_ready, N1 * (b + 1))
                for n in range(N2):
                    for k in range(N1):
                        last = nc.tensor.matmul(mlp_ps[n % 2][:, 0:BLOCK], w2_sb[:, k, n * P:(n + 1) * P],
                                                h1[:, k, :], start=(k == 0), stop=(k == N1 - 1))
                    last.then_inc(l2_done, 1)

            def layer3(b):
                pe.wait_ge(h2_ready, N2 * (b + 1))
                for k in range(N2):
                    last = nc.tensor.matmul(mlp_ps[0][0:1, 0:BLOCK], w3_sb[:, k:k + 1], h2[:, k, :],
                                            start=(k == 0), stop=(k == N2 - 1))
                last.then_inc(l3_done, 1)

            pe.wait_ge(ident_set, 1)
            transpose_two(0, 0, True)
            for p in range(PAIRS):
                if p + 1 < PAIRS:
                    transpose_two(0, p + 1, True)
                dot_two(0, p, True)
            pe.wait_ge(weights_in, 32)
            pe.wait_ge(small_in, 48)
            with pe.Fori(1, NB) as b:
                transpose_two(b, 0, False)
                for p in range(PAIRS):
                    if p + 1 < PAIRS:
                        transpose_two(b, p + 1, False)
                    dot_two(b, p, False)
                    if p == PER_BATCH - 1:
                        layer1(b - 1)
                    if p == PER_BATCH:
                        layer2(b - 1)
                    if p == PER_BATCH + 1:
                        layer3(b - 1)
            pe.wait_ge(y_ready, NB - 1)
            layer1(NB - 1)
            layer2(NB - 1)
            layer3(NB - 1)


def kernel(**inputs):
    import concourse.bacc as bacc
    from concourse.bass_utils import run_bass_kernel_spmd

    a = {k: np.asarray(v) for k, v in inputs.items()}
    ids, dense = a["ids"], a["dense_ctx"]
    B, F = ids.shape
    tables = [a[f"tbl_{f}"] for f in range(F)]
    nb = B // BLOCK

    by_group = ids.reshape(nb, GROUP, GROUPS, F).transpose(1, 3, 0, 2).reshape(P, nb * GROUPS)
    base = np.cumsum([0] + [t.shape[0] for t in tables[:-1]]).astype(np.int32)

    W1 = a["W_top1"]
    H1 = W1.shape[1]
    w1 = np.zeros((QUADS, Q, JJ, H1), W1.dtype)
    iu, ju = np.triu_indices(F, k=1)
    w1[ju // JJ, iu, ju % JJ] = W1[:len(iu)]
    nd = dense.shape[1]
    w1[np.arange(nd) // JJ, Q - 1, np.arange(nd) % JJ] = W1[len(iu):]

    arrays = {
        "table": np.concatenate(tables, axis=0),
        "ids": by_group,
        "base": np.tile(base, GROUP)[:, None],
        "dense": dense.reshape(nb, BLOCK, nd // JJ, JJ).transpose(0, 2, 3, 1),
        "w1": w1.reshape(P, JJ, H1),
        "b1": a["b_top1"].reshape(-1, P).T,
        "w2": a["W_top2"].reshape(H1 // P, P, -1).transpose(1, 0, 2),
        "b2": a["b_top2"].reshape(-1, P).T,
        "w3": a["W_top3"].reshape(-1, P).T,
    }
    arrays = {k: np.ascontiguousarray(v) for k, v in arrays.items()}
    nc = bacc.Bacc("TRN2", target_bir_lowering=False, num_devices=1)
    args = [nc.dram_tensor(k, v.shape, mybir.dt.from_np(v.dtype), kind="ExternalInput").ap() for k, v in arrays.items()]
    args.append(nc.dram_tensor("out", (1, B), F32, kind="ExternalOutput").ap())
    build_tower(nc, *args)
    got = run_bass_kernel_spmd(nc, [arrays], core_ids=[0]).results[0]["out"]
    return got.reshape(B, 1)
```

```python
from contextlib import ExitStack

import numpy as np

import concourse.bass as bass
from concourse import mybir

F32 = mybir.dt.float32
F32R = mybir.dt.float32r
I32 = mybir.dt.int32
ALU = mybir.AluOpType
ACT = mybir.ActivationFunctionType

P = 128
Q = 32
QUADS = P // Q
N_FIELDS = 32
LOOKED_UP = 4
GROUP = P // N_FIELDS
BATCH = 8
HALF = BATCH // 2
SAMPLES = BATCH * GROUP
BLOCK = 128
BATCHES = BLOCK // SAMPLES
UNIT = 2
PER_GATHER = P // SAMPLES
GATHERS = (N_FIELDS - LOOKED_UP) // PER_GATHER
FILLS = (GATHERS + 1) // 2
SLOTS = BATCHES * GATHERS
JJ = N_FIELDS // QUADS
ACT_SAMPLES = 1
FILL_BANKS = [f % 3 for f in range(15)] + [1]
ROUND = {"layer1": [2, 3, 4, 6, 7, 8, 9, 10], "relu1": 11, "layer2": [13, 14], "relu2": 15, "layer3": 15}
LAST_ROUND = {"layer1": [1, 2, 3, 4, 5, 6, 7, 7], "relu1": None, "layer2": [], "relu2": None, "layer3": None}
AHEAD = 2
LAG = 2
RING = 2 * AHEAD


def build_tower(nc, table, ids, small_tables, small_ids, chunk_rows, dense, w1, w1d, b1, w2, b2, w3, out):
    D = table.shape[1]
    DC = D // P
    B = out.shape[1]
    NB = B // BLOCK
    NM = NB * BATCHES
    H1, H2 = w1.shape[2], w2.shape[2]
    N1, N2 = H1 // P, H2 // P
    KR, CHUNKS = chunk_rows.shape
    assert N_FIELDS == Q and GROUP == QUADS and DC == 2 and CHUNKS % 2 == 0
    TWOS = LOOKED_UP * CHUNKS // 2
    assert FILLS == BATCH // 2 == LOOKED_UP and BATCHES == 2 * UNIT and len(FILL_BANKS) == BATCHES * FILLS == TWOS

    with ExitStack() as ctx:
        def sb(name, shape, dt=F32):
            return ctx.enter_context(nc.sbuf_tensor(name, shape, dt))

        def bank(name):
            return ctx.enter_context(nc.psum_tensor(name, [P, 512], F32))

        def sem(name):
            return ctx.enter_context(nc.semaphore(name))

        ids_sb = sb("ids_sb", [P, 2, NM * GATHERS], I32)
        row_ids = sb("row_ids", [P, NM * GATHERS], I32)
        ident = sb("ident", [P, P])
        small_ids_sb = sb("small_ids_sb", [KR, 2, B], I32)
        chunk_rows_sb = sb("chunk_rows_sb", [KR, CHUNKS])
        small_sb = sb("small_sb", [KR, 2, CHUNKS, D])
        high = sb("high", [KR, RING, D], F32R)
        low = sb("low", [KR, RING, D], F32R)
        one_hot = sb("one_hot", [KR, RING, B], F32R)
        kept = sb("kept", [P, DC, B, LOOKED_UP])
        rows = sb("rows", [P, SLOTS, D])
        xt = sb("xt", [P, BATCHES, DC, 2, SAMPLES, N_FIELDS], F32R)
        summed = sb("summed", [P, 2, UNIT * BATCH, P])
        pairs = sb("pairs", [P, NB, JJ, BLOCK])
        dense_sb = sb("dense_sb", [dense.shape[0], B])
        w1d_sb = sb("w1d_sb", [dense.shape[0], H1])
        w1_sb = sb("w1_sb", [P, JJ, H1])
        w2_sb = sb("w2_sb", [P, N1, H2])
        w3_sb = sb("w3_sb", [P, N2])
        b1_sb = sb("b1_sb", [P, N1])
        b2_sb = sb("b2_sb", [P, N2])
        h1 = sb("h1", [P, N1, BLOCK])
        h2 = sb("h2", [P, N2, BLOCK])
        y = sb("y", [1, B])

        xt_ps = [bank(f"xt_ps{n}") for n in range(3)]
        dots_ps = [ctx.enter_context(nc.psum_tensor(f"dots_ps{n}", [P, HALF, 2, P], F32)) for n in range(2)]
        found_ps = [[dots_ps[n][:, c * 2:(c + 1) * 2, :, :].rearrange("p g h s -> p (g h s)") for c in range(DC)]
                    for n in range(2)]
        mlp_ps = bank("mlp_ps")
        loop_ps = [mlp_ps[:, n * BLOCK:(n + 1) * BLOCK] for n in range(N1)]
        last_l1_ps = [ps[:, 0:BLOCK] for ps in (*xt_ps, mlp_ps)]
        last_l2_ps = [ps[:, 0:BLOCK] for ps in found_ps[0]]
        last_l3_ps = found_ps[1][0][0:1, 0:BLOCK]

        ids_in = sem("ids_in")
        small_in = [[sem(f"small_in{k}_{c}") for c in range(0, CHUNKS, 2)] for k in range(LOOKED_UP)]
        small_ids_in = [sem(f"small_ids_in{k}") for k in range(LOOKED_UP)]
        chunk_rows_in = sem("chunk_rows_in")
        weights_in = sem("weights_in")
        biases_in = sem("biases_in")
        ident_zeroed = sem("ident_zeroed")
        ident_set = sem("ident_set")
        ids_ready = sem("ids_ready")
        high_ready = sem("high_ready")
        low_ready = sem("low_ready")
        one_hot_ready = sem("one_hot_ready")
        chunk_used = sem("chunk_used")
        found_kept = sem("found_kept")
        gathered = [sem(f"gathered{n}") for n in range(SLOTS)]
        transposed = sem("transposed")
        a_ready = sem("a_ready")
        b_ready = sem("b_ready")
        kept_a_ready = sem("kept_a_ready")
        kept_b_ready = sem("kept_b_ready")
        dots_done = sem("dots_done")
        aa_taken = sem("aa_taken")
        dots_taken = sem("dots_taken")
        moved_act = sem("moved_act")
        moved_dve = sem("moved_dve")
        l1_done = sem("l1_done")
        h1_ready = sem("h1_ready")
        l2_done = sem("l2_done")
        h2_ready = sem("h2_ready")
        l3_done = sem("l3_done")
        y_ready = sem("y_ready")
        stored = sem("stored")

        def earlier(b, n, by):
            return (b, n - by) if n >= by else (b - 1, n - by + BATCHES)

        def before_first(b):
            return isinstance(b, int) and b < 0

        def is_first(b):
            return isinstance(b, int) and b == 0

        def xt_fill(n, part, u):
            fields = min(2, GATHERS - 2 * u) * PER_GATHER
            at = 2 * PER_GATHER * u
            return xt[:, n, :, part, :, at:at + fields].rearrange("d c s f -> d c f s"), fields

        def fill_ps(n, u, fields):
            ps = xt_ps[FILL_BANKS[n * FILLS + u]][:]
            return ps.rearrange("d (c f s) -> d c f s", c=DC, s=SAMPLES)[:, :, 0:fields, :]

        def products(n, h, product):
            at = (n % UNIT) * BATCH + h * HALF
            return summed[:, n // UNIT, at:at + HALF, :], dots_ps[h][:, :, product, :]

        def unit_to_move(b, n, u):
            if u == 0:
                b, n = earlier(b, n, 1)
            if n == 1:
                b, unit = b - 1, 1
            elif n == 3:
                unit = 0
            else:
                return None
            return None if before_first(b) else (b, unit, (u - 1) % FILLS)

        def moves(b, unit, of, piece, pieces):
            todo = []
            for s in (range(ACT_SAMPLES), range(ACT_SAMPLES, GROUP))[of]:
                for q in range(QUADS):
                    col = s * Q + unit * UNIT * BATCH
                    to = pairs[Q * q:Q * (q + 1), b, :, col:col + UNIT * BATCH]
                    square = summed[Q * s:Q * (s + 1), unit, :, Q * s + JJ * q:Q * s + JJ * (q + 1)]
                    todo.append((to, square.rearrange("i g j -> i j g")))
            return todo[piece * len(todo) // pieces:(piece + 1) * len(todo) // pieces]

        block = ctx.enter_context(nc.Block())

        @block.sync
        def _(sp):
            sp.dma_start(ids_sb[:], ids).then_inc(ids_in, 16)
            for k in range(LOOKED_UP):
                if k >= 2:
                    sp.wait_ge(one_hot_ready, (k - 1) * CHUNKS)
                    sp.wait_ge(high_ready, (k - 1) * CHUNKS // 2)
                    sp.wait_ge(low_ready, (k - 1) * CHUNKS // 2)
                if k:
                    sp.dma_start(small_ids_sb[:, k % 2, :],
                                 small_ids[:, k, :].to_broadcast([KR, B])).then_inc(small_ids_in[k], 16)
                for c in range(0, CHUNKS, 2):
                    sp.dma_start(small_sb[:, k % 2, c:c + 2, :],
                                 small_tables[k][:, c:c + 2, :]).then_inc(small_in[k][c // 2], 16)
            for to, source in ((b1_sb, b1), (b2_sb, b2), (w3_sb, w3)):
                sp.dma_start(to[:], source).then_inc(biases_in, 16)
            for j in range(JJ):
                sp.dma_start(w1_sb[:, j, :], w1[:, j, :]).then_inc(weights_in, 16)
            sp.dma_start(w1d_sb[:], w1d).then_inc(weights_in, 16)
            sp.dma_start(w2_sb[:], w2).then_inc(weights_in, 16)
            sp.dma_start(dense_sb[:], dense).then_inc(weights_in, 16)
            sp.wait_ge(y_ready, NB)
            sp.dma_start(out, y[:]).then_inc(stored, 16)
            sp.wait_ge(stored, 16)

        @block.gpsimd
        def _(pool):
            nc.gpsimd.memset(ident[:], 0.0).then_inc(ident_zeroed, 1)
            pool.wait_ge(ident_zeroed, 1)
            nc.gpsimd.affine_select(out=ident[:], in_=ident[:], compare_op=ALU.not_equal, fill=1.0, base=0,
                                    pattern=[[-1, P]], channel_multiplier=1).then_inc(ident_set, 1)
            pool.wait_ge(ids_ready, 1)
            for m in range(NM):
                for t in range(GATHERS):
                    slot = m % BATCHES * GATHERS + t
                    if m >= BATCHES and t % 2 == 0:
                        pool.wait_ge(transposed, (m - BATCHES) * FILLS + t // 2 + 1)
                    nc.gpsimd.indirect_dma_start(
                        rows[:, slot, :], None, table,
                        bass.IndirectOffsetOnAxis(ap=row_ids[:, m * GATHERS + t:m * GATHERS + t + 1], axis=0)).then_inc(gathered[slot], 16)

        @block.vector
        def _(dve):
            dve.wait_ge(ids_in, 16)
            nc.vector.tensor_tensor(row_ids[:], ids_sb[:, 0, :], ids_sb[:, 1, :], ALU.add).then_inc(ids_ready, 1)
            def take_b(b, n, u):
                dve.wait_ge(a_ready, b * BATCHES * FILLS + (n * FILLS + u + 1))
                to, fields = xt_fill(n, 1, u)
                nc.vector.tensor_tensor(to, fill_ps(n, u, fields), xt_fill(n, 0, u)[0],
                                        ALU.subtract).then_inc(b_ready, 1)

            def take_kept_b(b, n):
                dve.wait_ge(kept_a_ready, b * BATCHES + (n + 1))
                nc.vector.tensor_tensor(xt[:, n, :, 1, :, N_FIELDS - LOOKED_UP:],
                                        kept[:, :, bass.ds((b * BATCHES + n) * SAMPLES, SAMPLES), :],
                                        xt[:, n, :, 0, :, N_FIELDS - LOOKED_UP:],
                                        ALU.subtract).then_inc(kept_b_ready, 1)

            def take_dots(b, n, h):
                dve.wait_ge(aa_taken, b * BATCHES * 2 + (2 * n + h + 1))
                to, ab = products(n, h, 1)
                nc.vector.tensor_tensor(to, ab, to, ALU.add).then_inc(dots_taken, 1)

            def move(b, unit, part):
                if part == 0:
                    dve.wait_ge(dots_taken, b * BATCHES * 2 + (unit + 1) * UNIT * 2)
                for to, source in moves(b, unit, 1, part, FILLS):
                    last = nc.vector.tensor_copy(to, source)
                if part == FILLS - 1:
                    last.then_inc(moved_dve, 1)

            def step(b, n):
                for u in range(FILLS):
                    take_b(b, n, u)
                    if u == 0 and not before_first(earlier(b, n, 2)[0]):
                        take_dots(*earlier(b, n, 2), 1)
                    if u == 2:
                        take_dots(*earlier(b, n, 1), 0)
                    if u == 3:
                        take_kept_b(b, n)
                    if unit_to_move(b, n, u):
                        move(*unit_to_move(b, n, u))

            def prepare(two):
                for i in range(2 * two, 2 * two + 2):
                    k, c = divmod(i, CHUNKS)
                    if c == 0:
                        dve.wait_ge(small_ids_in[k], 16)
                    if i >= RING:
                        dve.wait_ge(chunk_used, i - RING + 1)
                    nc.vector.tensor_scalar(one_hot[:, i % RING, :], small_ids_sb[:, k % 2, :], chunk_rows_sb[:, c:c + 1],
                                            None, ALU.is_equal).then_inc(one_hot_ready, 1)
                dve.wait_ge(high_ready, two + 1)
                at = (i - 1) % RING
                nc.vector.tensor_tensor(low[:, at:at + 2, :], small_sb[:, k % 2, c - 1:c + 1, :],
                                        high[:, at:at + 2, :], ALU.subtract).then_inc(low_ready, 1)

            dve.wait_ge(chunk_rows_in, 16)
            for two in range(AHEAD):
                prepare(two)
            for two in range(TWOS + LAG):
                if two + AHEAD < TWOS:
                    prepare(two + AHEAD)
                if two == TWOS:
                    take_kept_b(0, 0)
                if two >= LAG:
                    take_b(0, *divmod(two - LAG, FILLS))
            for n in range(1, BATCHES):
                take_kept_b(0, n)
            take_dots(0, 0, 0)
            take_dots(0, 0, 1)
            for u in range(FILLS):
                take_b(1, 0, u)
                take_dots(0, 1 + u // 2, u % 2)
                if u:
                    move(0, 0, u - 1)
            take_kept_b(1, 0)
            take_dots(0, 3, 0)
            move(0, 0, FILLS - 1)
            step(1, 1)
            with dve.Fori(1, NB - 1) as b:
                for n in range(2, BATCHES + 2):
                    step(b + n // BATCHES, n % BATCHES)
            step(NB - 1, 2)
            step(NB - 1, 3)
            move(NB - 1, 0, FILLS - 1)
            take_dots(NB - 1, BATCHES - 2, 1)
            take_dots(NB - 1, BATCHES - 1, 0)
            take_dots(NB - 1, BATCHES - 1, 1)
            for part in range(FILLS):
                move(NB - 1, 1, part)

        @block.scalar
        def _(act):
            act.dma_start(small_ids_sb[:, 0, :], small_ids[:, 0, :].to_broadcast([KR, B])).then_inc(small_ids_in[0], 16)
            act.dma_start(chunk_rows_sb[:], chunk_rows).then_inc(chunk_rows_in, 16)

            def keep_found(k):
                act.wait_ge(chunk_used, (k + 1) * CHUNKS)
                for c in range(DC):
                    last = nc.scalar.copy(kept[:, c, :, k], found_ps[k % 2][c])
                last.then_inc(found_kept, 1)

            def take_a(b, n, u):
                act.wait_ge(transposed, b * BATCHES * FILLS + (n * FILLS + u + 1))
                to, fields = xt_fill(n, 0, u)
                nc.scalar.copy(to, fill_ps(n, u, fields)).then_inc(a_ready, 1)

            def take_aa(b, n, h):
                act.wait_ge(dots_done, b * BATCHES * 2 + (2 * n + h + 1))
                if h == 0 and n % UNIT == 0 and not is_first(b):
                    act.wait_ge(moved_dve, 2 * b + (n // UNIT - 1))
                    act.wait_ge(moved_act, 2 * b + (n // UNIT - 1))
                to, aa = products(n, h, 0)
                nc.scalar.mul(to, aa, 0.5).then_inc(aa_taken, 1)

            def take_kept_a(b, n):
                nc.scalar.copy(xt[:, n, :, 0, :, N_FIELDS - LOOKED_UP:],
                               kept[:, :, bass.ds((b * BATCHES + n) * SAMPLES, SAMPLES), :]
                               ).then_inc(kept_a_ready, 1)

            def move(b, unit, part):
                if part == 1:
                    act.wait_ge(dots_taken, b * BATCHES * 2 + (unit + 1) * UNIT * 2)
                for to, source in moves(b, unit, 0, part - 1, FILLS - 1) if part else ():
                    last = nc.scalar.copy(to, source)
                if part == FILLS - 1:
                    last.then_inc(moved_act, 1)

            def relu1(banks, n):
                nc.scalar.activation(h1[:, n, :], banks[n], ACT.Relu, bias=b1_sb[:, n:n + 1]).then_inc(h1_ready, 1)

            def relu2(b, banks):
                act.wait_ge(l2_done, b + 1)
                for n in range(N2):
                    nc.scalar.activation(h2[:, n, :], banks[n], ACT.Relu, bias=b2_sb[:, n:n + 1]).then_inc(h2_ready, 1)

            def keep_y(b, ps):
                act.wait_ge(l3_done, b + 1)
                nc.scalar.copy(y[:, bass.ds(b * BLOCK, BLOCK)], ps).then_inc(y_ready, 1)

            def prepare(two):
                i = 2 * two
                k, c = divmod(i, CHUNKS)
                if i >= RING:
                    act.wait_ge(chunk_used, i + 2 - RING)
                act.wait_ge(small_in[k][c // 2], 16)
                nc.scalar.copy(high[:, i % RING:i % RING + 2, :],
                               small_sb[:, k % 2, c:c + 2, :]).then_inc(high_ready, 1)

            for two in range(AHEAD):
                prepare(two)
            for two in range(TWOS + LAG):
                if two % (CHUNKS // 2) == 0 and two:
                    keep_found(2 * two // CHUNKS - 1)
                if two == TWOS:
                    act.wait_ge(found_kept, LOOKED_UP)
                    take_kept_a(0, 0)
                if two + AHEAD < TWOS:
                    prepare(two + AHEAD)
                if two >= LAG:
                    take_a(0, *divmod(two - LAG, FILLS))
            for n in range(1, BATCHES):
                take_kept_a(0, n)
            act.wait_ge(biases_in, 48)

            def relu1_all(b):
                act.wait_ge(l1_done, N1 * (b + 1))
                for k in range(N1):
                    relu1(loop_ps, k)

            def mlp(b, at, schedule):
                if at == schedule["relu1"]:
                    relu1_all(b)
                if at == schedule["relu2"]:
                    relu2(b, loop_ps)
                    keep_y(b, loop_ps[0][0:1, :])

            def step(b, n, mlp_block=None, at=0, schedule=None):
                for u in range(FILLS):
                    take_a(b, n, u)
                    if u == 0 and not before_first(earlier(b, n, 2)[0]):
                        take_aa(*earlier(b, n, 2), 1)
                    if u == 2:
                        take_aa(*earlier(b, n, 1), 0)
                    if u == 1:
                        take_kept_a(b, n)
                    if schedule:
                        mlp(mlp_block, at + u, schedule)
                    if unit_to_move(b, n, u):
                        move(*unit_to_move(b, n, u))

            take_aa(0, 0, 0)
            take_aa(0, 0, 1)
            for u in range(FILLS):
                take_a(1, 0, u)
                take_aa(0, 1 + u // 2, u % 2)
                if u:
                    move(0, 0, u - 1)
            take_kept_a(1, 0)
            take_aa(0, 3, 0)
            move(0, 0, FILLS - 1)
            step(1, 1)
            with act.Fori(1, NB - 1) as b:
                for n in range(BATCHES):
                    step(b + (n + 2) // BATCHES, (n + 2) % BATCHES, b - 1, n * FILLS, ROUND)
            for n in range(2):
                step(NB - 1, n + 2, NB - 2, n * FILLS, LAST_ROUND)
            move(NB - 1, 0, FILLS - 1)
            take_aa(NB - 1, BATCHES - 2, 1)
            relu1_all(NB - 2)
            take_aa(NB - 1, BATCHES - 1, 0)
            take_aa(NB - 1, BATCHES - 1, 1)
            for part in range(FILLS):
                move(NB - 1, 1, part)
            relu2(NB - 2, loop_ps)
            keep_y(NB - 2, loop_ps[0][0:1, :])
            for k in range(N1):
                act.wait_ge(l1_done, (NB - 1) * N1 + k + 1)
                relu1(last_l1_ps, k)
            relu2(NB - 1, last_l2_ps)
            keep_y(NB - 1, last_l3_ps)

        @block.tensor
        def _(pe):
            def look_up(two):
                for i in range(2 * two, 2 * two + 2):
                    k, c = divmod(i, CHUNKS)
                    if c == 0 and k >= 2:
                        pe.wait_ge(found_kept, k - 1)
                    pe.wait_ge(one_hot_ready, i + 1)
                    if i % 2 == 0:
                        pe.wait_ge(high_ready, two + 1)
                        pe.wait_ge(low_ready, two + 1)
                    for part in (high, low):
                        for d in range(DC):
                            last = nc.tensor.matmul(
                                found_ps[k % 2][d], part[:, i % RING, d * P:(d + 1) * P], one_hot[:, i % RING, :],
                                start=(c == 0 and part is high), stop=(c == CHUNKS - 1 and part is low))
                    last.then_inc(chunk_used, 1)

            def fill(b, n, u):
                at_fill = n * FILLS + u
                ps = xt_ps[FILL_BANKS[at_fill]]
                if not (is_first(b) and at_fill < 3):
                    last_use = max(f - (f >= at_fill) * len(FILL_BANKS) for f in range(len(FILL_BANKS))
                                   if FILL_BANKS[f] == FILL_BANKS[at_fill])
                    pe.wait_ge(b_ready, b * BATCHES * FILLS + (last_use + 1))
                for t in range(2 * u, min(2 * u + 2, GATHERS)):
                    slot = n * GATHERS + t
                    pe.wait_ge(gathered[slot], 16 * (b + 1))
                    for c in range(DC):
                        at = (2 * c + t % 2) * P
                        last = nc.tensor.transpose(ps[:, at:at + P],
                                                   rows[:, slot, c * P:(c + 1) * P], ident[:])
                last.then_inc(transposed, 1)

            def dots(b, n, u):
                h = u // 2
                if u == 0:
                    pe.wait_ge(b_ready, b * BATCHES * FILLS + (n + 1) * FILLS)
                    pe.wait_ge(kept_b_ready, b * BATCHES + (n + 1))
                if u % 2 == 0 and not (is_first(b) and n == 0):
                    pe.wait_ge(dots_taken, b * BATCHES * 2 + (2 * n + h - 1))
                for g in range(2 * u, 2 * u + 2):
                    for c in range(DC):
                        x = xt[:, n, c, :, g * GROUP:(g + 1) * GROUP, :].rearrange("d h s f -> d h (s f)")
                        last = nc.tensor.matmul(dots_ps[h][:, g % HALF, :, :], x[:, 0, :], x,
                                                start=(c == 0), stop=(c == DC - 1))
                if u % 2 == 1:
                    last.then_inc(dots_done, 1)

            def layer1(b, n, half, banks):
                for j in range(half * JJ // 2, (half + 1) * JJ // 2):
                    nc.tensor.matmul(banks[n], w1_sb[:, j, n * P:(n + 1) * P], pairs[:, b, j, :],
                                     start=(j == 0), stop=False)
                if half:
                    nc.tensor.matmul(banks[n], w1d_sb[:, n * P:(n + 1) * P], dense_sb[:, bass.ds(b * BLOCK, BLOCK)],
                                     start=False, stop=True).then_inc(l1_done, 1)

            def layer2(n, k, banks):
                done = nc.tensor.matmul(banks[n], w2_sb[:, k, n * P:(n + 1) * P], h1[:, k, :],
                                        start=(k == 0), stop=(k == N1 - 1))
                if n == N2 - 1 and k == N1 - 1:
                    done.then_inc(l2_done, 1)

            def pairs_complete(b):
                pe.wait_ge(moved_dve, 2 * (b + 1))
                pe.wait_ge(moved_act, 2 * (b + 1))

            def layer3(b, ps):
                for k in range(N2):
                    pe.wait_ge(h2_ready, N2 * b + (k + 1))
                    last = nc.tensor.matmul(ps, w3_sb[:, k:k + 1], h2[:, k, :], start=(k == 0), stop=(k == N2 - 1))
                last.then_inc(l3_done, 1)

            def mlp(b, at, schedule):
                for i, when in enumerate(schedule["layer1"]):
                    if at == when:
                        if i == 0:
                            pairs_complete(b)
                            pe.wait_ge(a_ready, ((b + 1) * BATCHES + 2) * FILLS + 1)
                        layer1(b, i // 2, i % 2, loop_ps)
                for i, when in enumerate(schedule["layer2"]):
                    if at == when:
                        if i == 0:
                            pe.wait_ge(h1_ready, N1 * (b + 1))
                        for k in range(N1):
                            layer2(i, k, loop_ps)
                if at == schedule["layer3"]:
                    pe.wait_ge(h2_ready, N2 * (b + 1))
                    layer3(b, loop_ps[0][0:1, :])

            def step(b, n, mlp_block=None, at=0, schedule=None):
                for u in range(FILLS):
                    fill(b, n, u)
                    if u:
                        dots(*earlier(b, n, 1), u - 1)
                    elif not before_first(earlier(b, n, 2)[0]):
                        dots(*earlier(b, n, 2), FILLS - 1)
                    if schedule:
                        mlp(mlp_block, at + u, schedule)

            pe.wait_ge(ident_set, 1)
            for two in range(TWOS + LAG):
                if two < TWOS:
                    look_up(two)
                if two >= LAG:
                    fill(0, *divmod(two - LAG, FILLS))
            pe.wait_ge(found_kept, LOOKED_UP)
            for u in range(FILLS):
                dots(0, 0, u)
            for u in range(FILLS):
                fill(1, 0, u)
                dots(0, 1 + u // 2, 2 * (u % 2))
                dots(0, 1 + u // 2, 2 * (u % 2) + 1)
            for u in range(FILLS - 1):
                dots(0, 3, u)
            step(1, 1)
            pe.wait_ge(weights_in, 16 * (JJ + 3))
            with pe.Fori(1, NB - 1) as b:
                for n in range(BATCHES):
                    step(b + (n + 2) // BATCHES, (n + 2) % BATCHES, b - 1, n * FILLS, ROUND)
            for n in range(2):
                step(NB - 1, n + 2, NB - 2, n * FILLS, LAST_ROUND)
            dots(NB - 1, BATCHES - 2, FILLS - 1)
            for u in range(FILLS):
                dots(NB - 1, BATCHES - 1, u)
            pe.wait_ge(h1_ready, N1 * (NB - 1))
            for n in range(N2):
                for k in range(N1):
                    layer2(n, k, loop_ps)
            pe.wait_ge(h2_ready, N2 * (NB - 1))
            layer3(NB - 2, loop_ps[0][0:1, :])
            pairs_complete(NB - 1)
            for k in range(N1 + 1):
                if k < N1:
                    if last_l1_ps[k] is last_l1_ps[-1]:
                        pe.wait_ge(y_ready, NB - 1)
                    for half in range(2):
                        layer1(NB - 1, k, half, last_l1_ps)
                if k:
                    pe.wait_ge(h1_ready, (NB - 1) * N1 + k)
                    for n in range(N2):
                        layer2(n, k - 1, last_l2_ps)
            layer3(NB - 1, last_l3_ps)


def kernel(**inputs):
    import concourse.bacc as bacc
    from concourse.bass_utils import run_bass_kernel_spmd

    a = {k: np.asarray(v) for k, v in inputs.items()}
    ids, dense = a["ids"], a["dense_ctx"]
    B, F = ids.shape
    nb, nm = B // BLOCK, B // SAMPLES
    tables = [a[f"tbl_{f}"] for f in range(F)]

    by_size = sorted(range(F), key=lambda f: -tables[f].shape[0])
    order = sorted(by_size[:F - LOOKED_UP]) + sorted(by_size[F - LOOKED_UP:])
    gathered, looked_up = order[:F - LOOKED_UP], order[F - LOOKED_UP:]

    samples = np.arange(B).reshape(nb, GROUP, B // nb // GROUP).transpose(0, 2, 1).reshape(nm, SAMPLES)
    ids_m = ids[samples]
    per_gather = ids_m[:, :, gathered].reshape(nm, SAMPLES, GATHERS, PER_GATHER).transpose(3, 1, 0, 2)
    first_row = np.cumsum([0] + [tables[f].shape[0] for f in gathered[:-1]]).astype(np.int32)
    base = np.repeat(first_row.reshape(GATHERS, PER_GATHER).T, SAMPLES, axis=0)

    chunks = 8
    n_rows = tables[looked_up[0]].shape[0]
    kr = n_rows // chunks
    assert kr <= P and kr * chunks == n_rows and all(tables[f].shape[0] == n_rows for f in looked_up)

    W1 = a["W_top1"]
    H1 = W1.shape[1]
    row_of = np.zeros((F, F), np.int64)
    iu, ju = np.triu_indices(F, k=1)
    row_of[iu, ju] = row_of[ju, iu] = np.arange(len(iu))
    i, j = np.nonzero(1 - np.eye(F, dtype=np.int64))
    w1 = np.zeros((QUADS, Q, JJ, H1), W1.dtype)
    w1[j // JJ, i, j % JJ] = W1[row_of[np.array(order)[i], np.array(order)[j]]]

    arrays = {
        "table": np.concatenate([tables[f] for f in gathered], axis=0),
        "ids": np.stack([per_gather.reshape(P, -1), np.tile(base, (1, nm))], axis=1),
        "small_tables": np.stack([tables[f].reshape(kr, chunks, -1) for f in looked_up]),
        "small_ids": ids_m[:, :, looked_up].reshape(B, LOOKED_UP).T[None],
        "chunk_rows": np.arange(n_rows, dtype=np.float32).reshape(kr, chunks),
        "dense": dense.T,
        "w1": w1.reshape(P, JJ, H1),
        "w1d": W1[len(iu):],
        "b1": a["b_top1"].reshape(-1, P).T,
        "w2": a["W_top2"].reshape(H1 // P, P, -1).transpose(1, 0, 2),
        "b2": a["b_top2"].reshape(-1, P).T,
        "w3": a["W_top3"].reshape(-1, P).T,
    }
    arrays = {k: np.ascontiguousarray(v) for k, v in arrays.items()}
    nc = bacc.Bacc("TRN2", target_bir_lowering=False, num_devices=1)
    args = [nc.dram_tensor(k, v.shape, mybir.dt.from_np(v.dtype), kind="ExternalInput").ap() for k, v in arrays.items()]
    args.append(nc.dram_tensor("out", (1, B), F32, kind="ExternalOutput").ap())
    build_tower(nc, *args)
    got = run_bass_kernel_spmd(nc, [arrays], core_ids=[0]).results[0]["out"]
    return got.reshape(B, 1)
```

```python
from contextlib import ExitStack

import numpy as np

import concourse.bass as bass
from concourse import mybir

F32 = mybir.dt.float32
F32R = mybir.dt.float32r
I32 = mybir.dt.int32
ALU = mybir.AluOpType
ACT = mybir.ActivationFunctionType

P = 128
Q = 32
QUADS = P // Q
N_FIELDS = 32
LOOKED_UP = 4
GROUP = P // N_FIELDS
BATCH = 8
HALF = BATCH // 2
SAMPLES = BATCH * GROUP
BLOCK = 128
BATCHES = BLOCK // SAMPLES
UNIT = 2
PER_GATHER = P // SAMPLES
GATHERS = (N_FIELDS - LOOKED_UP) // PER_GATHER
FILLS = (GATHERS + 1) // 2
SLOTS = BATCHES * GATHERS
JJ = N_FIELDS // QUADS
PIECES = 4
ACT_MOVES = 4
LAST_ACT_MOVES = 6
FILL_BANKS = [f % 3 for f in range(15)] + [1]
ROUND = {"layer1": [2, 3, 4, 6, 7, 8, 9, 10], "relu1": 11, "layer2": [13, 14], "relu2": 15, "layer3": 15}
LAST_ROUND = {"layer1": [0, 1, 2, 3, 4, 5], "relu1": None, "layer2": [], "relu2": None, "layer3": None}
MOVES = [[], [0], [1, 2], [3]]
LAST_MOVES = [[0], [1, 2], [], []]
AHEAD = 2
LAG = 2
RING = 2 * AHEAD


def build_tower(nc, table, ids, small_tables, small_ids, chunk_rows, dense, w1, w1d, b1, w2, b2, w3, out):
    D = table.shape[1]
    DC = D // P
    B = out.shape[1]
    NB = B // BLOCK
    NM = NB * BATCHES
    H1, H2 = w1.shape[2], w2.shape[2]
    N1, N2 = H1 // P, H2 // P
    KR, CHUNKS = chunk_rows.shape
    assert N_FIELDS == Q and GROUP == QUADS and DC == 2 and CHUNKS % 2 == 0
    TWOS = LOOKED_UP * CHUNKS // 2
    assert FILLS == BATCH // 2 == LOOKED_UP and BATCHES == 2 * UNIT and len(FILL_BANKS) == BATCHES * FILLS == TWOS

    with ExitStack() as ctx:
        def sb(name, shape, dt=F32):
            return ctx.enter_context(nc.sbuf_tensor(name, shape, dt))

        def bank(name):
            return ctx.enter_context(nc.psum_tensor(name, [P, 512], F32))

        def sem(name):
            return ctx.enter_context(nc.semaphore(name))

        ids_sb = sb("ids_sb", [P, 2, NM * GATHERS], I32)
        row_ids = sb("row_ids", [P, NM * GATHERS], I32)
        ident = sb("ident", [P, P])
        small_ids_sb = sb("small_ids_sb", [KR, 2, B], I32)
        chunk_rows_sb = sb("chunk_rows_sb", [KR, CHUNKS])
        small_sb = sb("small_sb", [KR, 2, CHUNKS, D])
        high = sb("high", [KR, RING, D], F32R)
        low = sb("low", [KR, RING, D], F32R)
        one_hot = sb("one_hot", [KR, RING, B], F32R)
        kept = sb("kept", [P, DC, B, LOOKED_UP])
        rows = sb("rows", [P, SLOTS, D])
        xt = sb("xt", [P, BATCHES, DC, 2, SAMPLES, N_FIELDS], F32R)
        summed = sb("summed", [P, 2, UNIT * BATCH, P])
        pairs = sb("pairs", [P, NB, JJ, BLOCK])
        dense_sb = sb("dense_sb", [dense.shape[0], B])
        w1d_sb = sb("w1d_sb", [dense.shape[0], H1])
        w1_sb = sb("w1_sb", [P, JJ, H1])
        w2_sb = sb("w2_sb", [P, N1, H2])
        w3_sb = sb("w3_sb", [P, N2])
        b1_sb = sb("b1_sb", [P, N1])
        b2_sb = sb("b2_sb", [P, N2])
        h1 = sb("h1", [P, N1, BLOCK])
        h2 = sb("h2", [P, N2, BLOCK])
        y = sb("y", [1, B])

        xt_ps = [bank(f"xt_ps{n}") for n in range(3)]
        dots_ps = [ctx.enter_context(nc.psum_tensor(f"dots_ps{n}", [P, HALF, 2, P], F32)) for n in range(2)]
        found_ps = [[dots_ps[n][:, c * 2:(c + 1) * 2, :, :].rearrange("p g h s -> p (g h s)") for c in range(DC)]
                    for n in range(2)]
        mlp_ps = bank("mlp_ps")
        loop_ps = [mlp_ps[:, n * BLOCK:(n + 1) * BLOCK] for n in range(N1)]
        last_l1_ps = [ps[:, 0:BLOCK] for ps in (*xt_ps, mlp_ps)]
        last_l2_ps = [ps[:, 0:BLOCK] for ps in found_ps[0]]
        last_l3_ps = found_ps[1][0][0:1, 0:BLOCK]

        ids_in = sem("ids_in")
        small_in = [[sem(f"small_in{k}_{c}") for c in range(0, CHUNKS, 2)] for k in range(LOOKED_UP)]
        small_ids_in = [sem(f"small_ids_in{k}") for k in range(LOOKED_UP)]
        chunk_rows_in = sem("chunk_rows_in")
        weights_in = sem("weights_in")
        biases_in = sem("biases_in")
        ident_zeroed = sem("ident_zeroed")
        ident_set = sem("ident_set")
        ids_ready = sem("ids_ready")
        high_ready = sem("high_ready")
        low_ready = sem("low_ready")
        one_hot_ready = sem("one_hot_ready")
        chunk_used = sem("chunk_used")
        found_kept = sem("found_kept")
        gathered = [sem(f"gathered{n}") for n in range(SLOTS)]
        transposed = sem("transposed")
        a_ready = sem("a_ready")
        b_ready = sem("b_ready")
        kept_a_ready = sem("kept_a_ready")
        kept_b_ready = sem("kept_b_ready")
        dots_done = sem("dots_done")
        aa_taken = sem("aa_taken")
        dots_taken = sem("dots_taken")
        moved_act = sem("moved_act")
        moved_dve = sem("moved_dve")
        l1_done = sem("l1_done")
        h1_ready = sem("h1_ready")
        l2_done = sem("l2_done")
        h2_ready = sem("h2_ready")
        l3_done = sem("l3_done")
        y_ready = sem("y_ready")
        stored = sem("stored")

        def earlier(b, n, by):
            return (b, n - by) if n >= by else (b - 1, n - by + BATCHES)

        def is_first(b):
            return isinstance(b, int) and b == 0

        def xt_fill(n, part, u):
            fields = min(2, GATHERS - 2 * u) * PER_GATHER
            at = 2 * PER_GATHER * u
            return xt[:, n, :, part, :, at:at + fields].rearrange("d c s f -> d c f s"), fields

        def fill_ps(n, u, fields):
            ps = xt_ps[FILL_BANKS[n * FILLS + u]][:]
            return ps.rearrange("d (c f s) -> d c f s", c=DC, s=SAMPLES)[:, :, 0:fields, :]

        def products(n, h, product):
            at = (n % UNIT) * BATCH + h * HALF
            return summed[:, n // UNIT, at:at + HALF, :], dots_ps[h][:, :, product, :]

        def to_move(b, n, u):
            if n % UNIT == 0:
                return ()
            is_last = isinstance(b, int) and (b, n) == (NB - 1, BATCHES - 1)
            of, unit = (b, 0) if n == 3 else (b - 1, 1)
            return [(of, unit, piece) for piece in (LAST_MOVES if is_last else MOVES)[u]]

        def moves(b, unit, engine, piece, pieces):
            todo = []
            for s in range(GROUP):
                for q in range(QUADS):
                    col = s * Q + unit * UNIT * BATCH
                    to = pairs[Q * q:Q * (q + 1), b, :, col:col + UNIT * BATCH]
                    square = summed[Q * s:Q * (s + 1), unit, :, Q * s + JJ * q:Q * s + JJ * (q + 1)]
                    todo.append((to, square.rearrange("i g j -> i j g")))
            is_last = isinstance(b, int) and (b, unit) == (NB - 1, 1)
            n_act = LAST_ACT_MOVES if is_last else ACT_MOVES
            todo = (todo[:n_act], todo[n_act:])[engine]
            return todo[piece * len(todo) // pieces:(piece + 1) * len(todo) // pieces]

        block = ctx.enter_context(nc.Block())

        @block.sync
        def _(sp):
            sp.dma_start(ids_sb[:], ids).then_inc(ids_in, 16)
            for k in range(LOOKED_UP):
                if k >= 2:
                    sp.wait_ge(one_hot_ready, (k - 1) * CHUNKS)
                    sp.wait_ge(high_ready, (k - 1) * CHUNKS // 2)
                    sp.wait_ge(low_ready, (k - 1) * CHUNKS // 2)
                if k:
                    sp.dma_start(small_ids_sb[:, k % 2, :],
                                 small_ids[:, k, :].to_broadcast([KR, B])).then_inc(small_ids_in[k], 16)
                for c in range(0, CHUNKS, 2):
                    sp.dma_start(small_sb[:, k % 2, c:c + 2, :],
                                 small_tables[k][:, c:c + 2, :]).then_inc(small_in[k][c // 2], 16)
            for to, source in ((b1_sb, b1), (b2_sb, b2), (w3_sb, w3)):
                sp.dma_start(to[:], source).then_inc(biases_in, 16)
            for j in range(JJ):
                sp.dma_start(w1_sb[:, j, :], w1[:, j, :]).then_inc(weights_in, 16)
            sp.dma_start(w1d_sb[:], w1d).then_inc(weights_in, 16)
            sp.dma_start(w2_sb[:], w2).then_inc(weights_in, 16)
            sp.dma_start(dense_sb[:], dense).then_inc(weights_in, 16)
            sp.wait_ge(y_ready, NB)
            sp.dma_start(out, y[:]).then_inc(stored, 16)
            sp.wait_ge(stored, 16)

        @block.gpsimd
        def _(pool):
            nc.gpsimd.memset(ident[:], 0.0).then_inc(ident_zeroed, 1)
            pool.wait_ge(ident_zeroed, 1)
            nc.gpsimd.affine_select(out=ident[:], in_=ident[:], compare_op=ALU.not_equal, fill=1.0, base=0,
                                    pattern=[[-1, P]], channel_multiplier=1).then_inc(ident_set, 1)
            pool.wait_ge(ids_ready, 1)
            for m in range(NM):
                for t in range(GATHERS):
                    slot = m % BATCHES * GATHERS + t
                    if m >= BATCHES and t % 2 == 0:
                        pool.wait_ge(transposed, (m - BATCHES) * FILLS + t // 2 + 1)
                    nc.gpsimd.indirect_dma_start(
                        rows[:, slot, :], None, table,
                        bass.IndirectOffsetOnAxis(ap=row_ids[:, m * GATHERS + t:m * GATHERS + t + 1], axis=0)).then_inc(gathered[slot], 16)

        @block.vector
        def _(dve):
            dve.wait_ge(ids_in, 16)
            nc.vector.tensor_tensor(row_ids[:], ids_sb[:, 0, :], ids_sb[:, 1, :], ALU.add).then_inc(ids_ready, 1)
            def take_b(b, n, u):
                dve.wait_ge(a_ready, b * BATCHES * FILLS + (n * FILLS + u + 1))
                to, fields = xt_fill(n, 1, u)
                nc.vector.tensor_tensor(to, fill_ps(n, u, fields), xt_fill(n, 0, u)[0],
                                        ALU.subtract).then_inc(b_ready, 1)

            def take_kept_b(b, n):
                dve.wait_ge(kept_a_ready, b * BATCHES + (n + 1))
                nc.vector.tensor_tensor(xt[:, n, :, 1, :, N_FIELDS - LOOKED_UP:],
                                        kept[:, :, bass.ds((b * BATCHES + n) * SAMPLES, SAMPLES), :],
                                        xt[:, n, :, 0, :, N_FIELDS - LOOKED_UP:],
                                        ALU.subtract).then_inc(kept_b_ready, 1)

            def take_dots(b, n, h):
                dve.wait_ge(aa_taken, b * BATCHES * 2 + (2 * n + h + 1))
                to, ab = products(n, h, 1)
                nc.vector.tensor_tensor(to, ab, to, ALU.add).then_inc(dots_taken, 1)

            def move(b, unit, piece):
                if piece == 0:
                    dve.wait_ge(dots_taken, b * BATCHES * 2 + (unit + 1) * UNIT * 2)
                for to, source in moves(b, unit, 1, piece, PIECES):
                    last = nc.vector.tensor_copy(to, source)
                if piece == PIECES - 1:
                    last.then_inc(moved_dve, 1)

            def step(b, n):
                for u in range(FILLS):
                    take_b(b, n, u)
                    if u == 0:
                        take_dots(*earlier(b, n, 2), 1)
                    if u == 2:
                        take_dots(*earlier(b, n, 1), 0)
                    for what in to_move(b, n, u):
                        move(*what)
                    if u == 1:
                        take_kept_b(b, n)

            def prepare(two):
                for i in range(2 * two, 2 * two + 2):
                    k, c = divmod(i, CHUNKS)
                    if c == 0:
                        dve.wait_ge(small_ids_in[k], 16)
                    if i >= RING:
                        dve.wait_ge(chunk_used, i - RING + 1)
                    nc.vector.tensor_scalar(one_hot[:, i % RING, :], small_ids_sb[:, k % 2, :], chunk_rows_sb[:, c:c + 1],
                                            None, ALU.is_equal).then_inc(one_hot_ready, 1)
                dve.wait_ge(high_ready, two + 1)
                at = (i - 1) % RING
                nc.vector.tensor_tensor(low[:, at:at + 2, :], small_sb[:, k % 2, c - 1:c + 1, :],
                                        high[:, at:at + 2, :], ALU.subtract).then_inc(low_ready, 1)

            dve.wait_ge(chunk_rows_in, 16)
            for two in range(AHEAD):
                prepare(two)
            for two in range(TWOS + LAG):
                if two + AHEAD < TWOS:
                    prepare(two + AHEAD)
                if two == TWOS:
                    take_kept_b(0, 0)
                if two >= LAG:
                    take_b(0, *divmod(two - LAG, FILLS))
            for n in range(1, BATCHES):
                take_kept_b(0, n)
            take_dots(0, 0, 0)
            take_dots(0, 0, 1)
            for u in range(FILLS):
                take_b(1, 0, u)
                take_dots(0, 1 + u // 2, u % 2)
                if u:
                    move(0, 0, u - 1)
            take_kept_b(1, 0)
            take_dots(0, 3, 0)
            move(0, 0, PIECES - 1)
            step(1, 1)
            with dve.Fori(1, NB - 1) as b:
                for n in range(BATCHES):
                    step(b + (n + 2) // BATCHES, (n + 2) % BATCHES)
            for n in range(2):
                step(NB - 1, n + 2)
            take_dots(NB - 1, BATCHES - 2, 1)
            move(NB - 1, 0, PIECES - 1)
            take_dots(NB - 1, BATCHES - 1, 0)
            take_dots(NB - 1, BATCHES - 1, 1)
            for piece in range(PIECES):
                move(NB - 1, 1, piece)
            dve.wait_ge(biases_in, 48)
            dve.wait_ge(l2_done, NB * N2)
            nc.vector.tensor_scalar(h2[:, N2 - 1, :], last_l2_ps[N2 - 1], b2_sb[:, N2 - 1:N2], 0.0,
                                    ALU.add, ALU.max).then_inc(h2_ready, 1)

        @block.scalar
        def _(act):
            act.dma_start(small_ids_sb[:, 0, :], small_ids[:, 0, :].to_broadcast([KR, B])).then_inc(small_ids_in[0], 16)
            act.dma_start(chunk_rows_sb[:], chunk_rows).then_inc(chunk_rows_in, 16)

            def keep_found(k):
                act.wait_ge(chunk_used, (k + 1) * CHUNKS)
                for c in range(DC):
                    last = nc.scalar.copy(kept[:, c, :, k], found_ps[k % 2][c])
                last.then_inc(found_kept, 1)

            def take_a(b, n, u):
                act.wait_ge(transposed, b * BATCHES * FILLS + (n * FILLS + u + 1))
                to, fields = xt_fill(n, 0, u)
                nc.scalar.copy(to, fill_ps(n, u, fields)).then_inc(a_ready, 1)

            def take_aa(b, n, h):
                act.wait_ge(dots_done, b * BATCHES * 2 + (2 * n + h + 1))
                if h == 0 and n % UNIT == 0 and not is_first(b):
                    act.wait_ge(moved_dve, 2 * b + (n // UNIT - 1))
                    act.wait_ge(moved_act, 2 * b + (n // UNIT - 1))
                to, aa = products(n, h, 0)
                nc.scalar.mul(to, aa, 0.5).then_inc(aa_taken, 1)

            def take_kept_a(b, n):
                nc.scalar.copy(xt[:, n, :, 0, :, N_FIELDS - LOOKED_UP:],
                               kept[:, :, bass.ds((b * BATCHES + n) * SAMPLES, SAMPLES), :]
                               ).then_inc(kept_a_ready, 1)

            def move(b, unit, piece):
                if piece == 1:
                    act.wait_ge(dots_taken, b * BATCHES * 2 + (unit + 1) * UNIT * 2)
                for to, source in moves(b, unit, 0, piece - 1, PIECES - 1) if piece else ():
                    last = nc.scalar.copy(to, source)
                if piece == PIECES - 1:
                    last.then_inc(moved_act, 1)

            def relu1(banks, n):
                nc.scalar.activation(h1[:, n, :], banks[n], ACT.Relu, bias=b1_sb[:, n:n + 1]).then_inc(h1_ready, 1)

            def relu2(b, banks, chunks=range(N2)):
                act.wait_ge(l2_done, b * N2 + chunks[-1] + 1)
                for n in chunks:
                    nc.scalar.activation(h2[:, n, :], banks[n], ACT.Relu, bias=b2_sb[:, n:n + 1]).then_inc(h2_ready, 1)

            def keep_y(b, ps):
                act.wait_ge(l3_done, b + 1)
                nc.scalar.copy(y[:, bass.ds(b * BLOCK, BLOCK)], ps).then_inc(y_ready, 1)

            def prepare(two):
                i = 2 * two
                k, c = divmod(i, CHUNKS)
                if i >= RING:
                    act.wait_ge(chunk_used, i + 2 - RING)
                act.wait_ge(small_in[k][c // 2], 16)
                nc.scalar.copy(high[:, i % RING:i % RING + 2, :],
                               small_sb[:, k % 2, c:c + 2, :]).then_inc(high_ready, 1)

            for two in range(AHEAD):
                prepare(two)
            for two in range(TWOS + LAG):
                if two + AHEAD < TWOS:
                    prepare(two + AHEAD)
                if two < TWOS and 2 * (two + 1) % CHUNKS == 0:
                    keep_found(2 * (two + 1) // CHUNKS - 1)
                if two == TWOS:
                    act.wait_ge(found_kept, LOOKED_UP)
                    take_kept_a(0, 0)
                if two >= LAG:
                    take_a(0, *divmod(two - LAG, FILLS))
            for n in range(1, BATCHES):
                take_kept_a(0, n)
            act.wait_ge(biases_in, 48)

            def relu1_all(b):
                act.wait_ge(l1_done, N1 * (b + 1))
                for k in range(N1):
                    relu1(loop_ps, k)

            def mlp(b, at, schedule):
                if at == schedule["relu1"]:
                    relu1_all(b)
                if at == schedule["relu2"]:
                    relu2(b, loop_ps)
                    keep_y(b, loop_ps[0][0:1, :])

            def step(b, n, mlp_block=None, at=0, schedule=None):
                for u in range(FILLS):
                    take_a(b, n, u)
                    if u == 0:
                        take_aa(*earlier(b, n, 2), 1)
                    if u == 2:
                        take_aa(*earlier(b, n, 1), 0)
                    if u == 1:
                        take_kept_a(b, n)
                    if schedule:
                        mlp(mlp_block, at + u, schedule)
                    for what in to_move(b, n, u):
                        move(*what)

            take_aa(0, 0, 0)
            take_aa(0, 0, 1)
            for u in range(FILLS):
                take_a(1, 0, u)
                take_aa(0, 1 + u // 2, u % 2)
                if u:
                    move(0, 0, u - 1)
            take_kept_a(1, 0)
            take_aa(0, 3, 0)
            move(0, 0, PIECES - 1)
            step(1, 1)
            with act.Fori(1, NB - 1) as b:
                for n in range(BATCHES):
                    step(b + (n + 2) // BATCHES, (n + 2) % BATCHES, b - 1, n * FILLS, ROUND)
            for n in range(2):
                step(NB - 1, n + 2, NB - 2, n * FILLS, LAST_ROUND)
            take_aa(NB - 1, BATCHES - 2, 1)
            move(NB - 1, 0, PIECES - 1)
            take_aa(NB - 1, BATCHES - 1, 0)
            relu1_all(NB - 2)
            take_aa(NB - 1, BATCHES - 1, 1)
            for piece in range(PIECES):
                move(NB - 1, 1, piece)
            relu2(NB - 2, loop_ps)
            keep_y(NB - 2, loop_ps[0][0:1, :])
            for k in range(N1):
                act.wait_ge(l1_done, (NB - 1) * N1 + k + 1)
                relu1(last_l1_ps, k)
            relu2(NB - 1, last_l2_ps, range(N2 - 1))
            keep_y(NB - 1, last_l3_ps)

        @block.tensor
        def _(pe):
            def look_up(two):
                for i in range(2 * two, 2 * two + 2):
                    k, c = divmod(i, CHUNKS)
                    if c == 0 and k >= 2:
                        pe.wait_ge(found_kept, k - 1)
                    pe.wait_ge(one_hot_ready, i + 1)
                    if i % 2 == 0:
                        pe.wait_ge(high_ready, two + 1)
                        pe.wait_ge(low_ready, two + 1)
                    for part in (high, low):
                        for d in range(DC):
                            last = nc.tensor.matmul(
                                found_ps[k % 2][d], part[:, i % RING, d * P:(d + 1) * P], one_hot[:, i % RING, :],
                                start=(c == 0 and part is high), stop=(c == CHUNKS - 1 and part is low))
                    last.then_inc(chunk_used, 1)

            def fill(b, n, u):
                at_fill = n * FILLS + u
                ps = xt_ps[FILL_BANKS[at_fill]]
                if not (is_first(b) and at_fill < 3):
                    last_use = max(f - (f >= at_fill) * len(FILL_BANKS) for f in range(len(FILL_BANKS))
                                   if FILL_BANKS[f] == FILL_BANKS[at_fill])
                    pe.wait_ge(b_ready, b * BATCHES * FILLS + (last_use + 1))
                for t in range(2 * u, min(2 * u + 2, GATHERS)):
                    slot = n * GATHERS + t
                    pe.wait_ge(gathered[slot], 16 * (b + 1))
                    for c in range(DC):
                        at = (2 * c + t % 2) * P
                        last = nc.tensor.transpose(ps[:, at:at + P],
                                                   rows[:, slot, c * P:(c + 1) * P], ident[:])
                last.then_inc(transposed, 1)

            def dots(b, n, u):
                h = u // 2
                if u == 0:
                    pe.wait_ge(b_ready, b * BATCHES * FILLS + (n + 1) * FILLS)
                    pe.wait_ge(kept_b_ready, b * BATCHES + (n + 1))
                if u % 2 == 0 and not (is_first(b) and n == 0):
                    pe.wait_ge(dots_taken, b * BATCHES * 2 + (2 * n + h - 1))
                for g in range(2 * u, 2 * u + 2):
                    for c in range(DC):
                        x = xt[:, n, c, :, g * GROUP:(g + 1) * GROUP, :].rearrange("d h s f -> d h (s f)")
                        last = nc.tensor.matmul(dots_ps[h][:, g % HALF, :, :], x[:, 0, :], x,
                                                start=(c == 0), stop=(c == DC - 1))
                if u % 2 == 1:
                    last.then_inc(dots_done, 1)

            def dense_part(b, n, banks, start=False):
                return nc.tensor.matmul(banks[n], w1d_sb[:, n * P:(n + 1) * P],
                                        dense_sb[:, bass.ds(b * BLOCK, BLOCK)], start=start, stop=not start)

            def pairs_part(b, n, columns, banks, start=True, stop=False):
                for j in columns:
                    done = nc.tensor.matmul(banks[n], w1_sb[:, j, n * P:(n + 1) * P], pairs[:, b, j, :],
                                            start=(start and j == 0), stop=(stop and j == JJ - 1))
                return done

            def layer1_half(b, i):
                pairs_part(b, i // 2, range(i % 2 * JJ // 2, (i % 2 + 1) * JJ // 2), loop_ps)
                if i % 2:
                    dense_part(b, i // 2, loop_ps).then_inc(l1_done, 1)

            def layer2(n, k, banks):
                done = nc.tensor.matmul(banks[n], w2_sb[:, k, n * P:(n + 1) * P], h1[:, k, :],
                                        start=(k == 0), stop=(k == N1 - 1))
                if k == N1 - 1:
                    done.then_inc(l2_done, 1)

            def pairs_complete(b):
                pe.wait_ge(moved_dve, 2 * (b + 1))
                pe.wait_ge(moved_act, 2 * (b + 1))

            def layer3(b, ps):
                pe.wait_ge(h2_ready, N2 * (b + 1))
                for k in range(N2):
                    last = nc.tensor.matmul(ps, w3_sb[:, k:k + 1], h2[:, k, :], start=(k == 0), stop=(k == N2 - 1))
                last.then_inc(l3_done, 1)

            def mlp(b, at, schedule):
                for i, when in enumerate(schedule["layer1"]):
                    if at == when:
                        if i == 0:
                            pairs_complete(b)
                            pe.wait_ge(a_ready, ((b + 1) * BATCHES + 2) * FILLS + 1)
                        layer1_half(b, i)
                for i, when in enumerate(schedule["layer2"]):
                    if at == when:
                        if i == 0:
                            pe.wait_ge(h1_ready, N1 * (b + 1))
                        for k in range(N1):
                            layer2(i, k, loop_ps)
                if at == schedule["layer3"]:
                    layer3(b, loop_ps[0][0:1, :])

            def step(b, n, mlp_block=None, at=0, schedule=None):
                for u in range(FILLS):
                    fill(b, n, u)
                    dots(*(earlier(b, n, 1) if u else earlier(b, n, 2)), (u - 1) % FILLS)
                    if schedule:
                        mlp(mlp_block, at + u, schedule)

            pe.wait_ge(ident_set, 1)
            for two in range(TWOS + LAG):
                if two < TWOS:
                    look_up(two)
                if two >= LAG:
                    fill(0, *divmod(two - LAG, FILLS))
            pe.wait_ge(found_kept, LOOKED_UP)
            for u in range(FILLS):
                dots(0, 0, u)
            for u in range(FILLS):
                fill(1, 0, u)
                dots(0, 1 + u // 2, 2 * (u % 2))
                dots(0, 1 + u // 2, 2 * (u % 2) + 1)
            for u in range(FILLS - 1):
                dots(0, 3, u)
            step(1, 1)
            pe.wait_ge(weights_in, 16 * (JJ + 3))
            with pe.Fori(1, NB - 1) as b:
                for n in range(BATCHES):
                    step(b + (n + 2) // BATCHES, (n + 2) % BATCHES, b - 1, n * FILLS, ROUND)
            for n in range(2):
                step(NB - 1, n + 2, NB - 2, n * FILLS, LAST_ROUND)
            m, last = NB - 2, NB - 1
            dots(last, BATCHES - 2, FILLS - 1)
            layer1_half(m, 2 * N1 - 2)
            dots(last, BATCHES - 1, 0)
            dots(last, BATCHES - 1, 1)
            layer1_half(m, 2 * N1 - 1)
            dots(last, BATCHES - 1, 2)
            dots(last, BATCHES - 1, 3)
            pe.wait_ge(h1_ready, N1 * last)
            for n in range(N2):
                for k in range(N1):
                    layer2(n, k, loop_ps)
            for k in range(N1 - 1):
                dense_part(last, k, last_l1_ps, start=True)
            pairs_complete(last)
            for k in range(N1 + 1):
                if k == 1:
                    layer3(m, loop_ps[0][0:1, :])
                if k == N1 - 1:
                    pe.wait_ge(y_ready, last)
                    dense_part(last, k, last_l1_ps, start=True)
                if k < N1:
                    pairs_part(last, k, range(JJ), last_l1_ps, start=False, stop=True).then_inc(l1_done, 1)
                if k:
                    pe.wait_ge(h1_ready, last * N1 + k)
                    for n in range(N2):
                        layer2(n, k - 1, last_l2_ps)
            layer3(last, last_l3_ps)


def kernel(**inputs):
    import concourse.bacc as bacc
    from concourse.bass_utils import run_bass_kernel_spmd

    a = {k: np.asarray(v) for k, v in inputs.items()}
    ids, dense = a["ids"], a["dense_ctx"]
    B, F = ids.shape
    nb, nm = B // BLOCK, B // SAMPLES
    tables = [a[f"tbl_{f}"] for f in range(F)]

    by_size = sorted(range(F), key=lambda f: -tables[f].shape[0])
    order = sorted(by_size[:F - LOOKED_UP]) + sorted(by_size[F - LOOKED_UP:])
    gathered, looked_up = order[:F - LOOKED_UP], order[F - LOOKED_UP:]

    samples = np.arange(B).reshape(nb, GROUP, B // nb // GROUP).transpose(0, 2, 1).reshape(nm, SAMPLES)
    ids_m = ids[samples]
    per_gather = ids_m[:, :, gathered].reshape(nm, SAMPLES, GATHERS, PER_GATHER).transpose(3, 1, 0, 2)
    first_row = np.cumsum([0] + [tables[f].shape[0] for f in gathered[:-1]]).astype(np.int32)
    base = np.repeat(first_row.reshape(GATHERS, PER_GATHER).T, SAMPLES, axis=0)

    chunks = 8
    n_rows = tables[looked_up[0]].shape[0]
    kr = n_rows // chunks
    assert kr <= P and kr * chunks == n_rows and all(tables[f].shape[0] == n_rows for f in looked_up)

    W1 = a["W_top1"]
    H1 = W1.shape[1]
    row_of = np.zeros((F, F), np.int64)
    iu, ju = np.triu_indices(F, k=1)
    row_of[iu, ju] = row_of[ju, iu] = np.arange(len(iu))
    i, j = np.nonzero(1 - np.eye(F, dtype=np.int64))
    w1 = np.zeros((QUADS, Q, JJ, H1), W1.dtype)
    w1[j // JJ, i, j % JJ] = W1[row_of[np.array(order)[i], np.array(order)[j]]]

    arrays = {
        "table": np.concatenate([tables[f] for f in gathered], axis=0),
        "ids": np.stack([per_gather.reshape(P, -1), np.tile(base, (1, nm))], axis=1),
        "small_tables": np.stack([tables[f].reshape(kr, chunks, -1) for f in looked_up]),
        "small_ids": ids_m[:, :, looked_up].reshape(B, LOOKED_UP).T[None],
        "chunk_rows": np.arange(n_rows, dtype=np.float32).reshape(kr, chunks),
        "dense": dense.T,
        "w1": w1.reshape(P, JJ, H1),
        "w1d": W1[len(iu):],
        "b1": a["b_top1"].reshape(-1, P).T,
        "w2": a["W_top2"].reshape(H1 // P, P, -1).transpose(1, 0, 2),
        "b2": a["b_top2"].reshape(-1, P).T,
        "w3": a["W_top3"].reshape(-1, P).T,
    }
    arrays = {k: np.ascontiguousarray(v) for k, v in arrays.items()}
    nc = bacc.Bacc("TRN2", target_bir_lowering=False, num_devices=1)
    args = [nc.dram_tensor(k, v.shape, mybir.dt.from_np(v.dtype), kind="ExternalInput").ap() for k, v in arrays.items()]
    args.append(nc.dram_tensor("out", (1, B), F32, kind="ExternalOutput").ap())
    build_tower(nc, *args)
    got = run_bass_kernel_spmd(nc, [arrays], core_ids=[0]).results[0]["out"]
    return got.reshape(B, 1)
```
